# Optimizing a Trainium2 kernel written in Bass

```python
import numpy as np
import jax
import jax.numpy as jnp

def _softmax(x, axis=-1):
    return jax.nn.softmax(x, axis=axis)

def _gelu(x):
    return jax.nn.gelu(x, approximate=True)

def _silu(x):
    return jax.nn.silu(x)

def _sigmoid(x):
    return jax.nn.sigmoid(x)

def _layernorm(x, axis=-1, eps=1e-05):
    m = jnp.mean(x, axis=axis, keepdims=True)
    v = jnp.var(x, axis=axis, keepdims=True)
    return (x - m) / jnp.sqrt(v + eps)

def _scatter_add(tgt, idx, src, axis=0):
    return tgt.at[idx].add(src)

def _segment_sum(src, seg, n):
    return jax.ops.segment_sum(src, seg, n)
kernel_name = 'mk_adaln_d2_jaxref_r8_fb4900'

def setup_inputs(seed: int=0):
    np.random.seed(seed)
    _w = jnp.asarray

    def _L0_attn_setup():
        import jax, jax.numpy as jnp
        import numpy as np
        D_MODEL, H, DK, DV = (128, 16, 64, 64)
        key = jax.random.key(seed)
        ks = jax.random.split(key, 9)
        s = lambda fan_in: 1.0 / np.sqrt(fan_in)
        return {'x': jax.random.normal(ks[0], (2, 256, D_MODEL), dtype=jnp.float32), 'Wq': jax.random.uniform(ks[1], (D_MODEL, H * DK), jnp.float32, -s(D_MODEL), s(D_MODEL)), 'bq': jax.random.uniform(ks[2], (H * DK,), jnp.float32, -s(D_MODEL), s(D_MODEL)), 'Wk': jax.random.uniform(ks[3], (D_MODEL, DK), jnp.float32, -s(D_MODEL), s(D_MODEL)), 'bk': jax.random.uniform(ks[4], (DK,), jnp.float32, -s(D_MODEL), s(D_MODEL)), 'Wv': jax.random.uniform(ks[5], (D_MODEL, DV), jnp.float32, -s(D_MODEL), s(D_MODEL)), 'bv': jax.random.uniform(ks[6], (DV,), jnp.float32, -s(D_MODEL), s(D_MODEL)), 'Wo': jax.random.uniform(ks[7], (H * DV, D_MODEL), jnp.float32, -s(H * DV), s(H * DV)), 'bo': jax.random.uniform(ks[8], (D_MODEL,), jnp.float32, -s(H * DV), s(H * DV))}
    _L0_attn_in = _L0_attn_setup()

    def _L0_ffn_setup():
        import jax, jax.numpy as jnp
        import numpy as np
        B, S, DIM = (4, 512, 128)
        BASE_COUPLING = 0.1
        NUM_CYCLES = 3

        def _gelu(x):
            return jax.nn.gelu(x, approximate=False)

        def _coupling_net(h, w1, b1, w2, b2, w3, b3, w4, b4):
            h = _gelu(h @ w1 + b1)
            h = _gelu(h @ w2 + b2)
            h = _gelu(h @ w3 + b3)
            return jax.nn.sigmoid(h @ w4 + b4)

        def _global_net(h, w1, b1, w2, b2, w3, b3):
            h = _gelu(h @ w1 + b1)
            h = _gelu(h @ w2 + b2)
            return jax.nn.sigmoid(h @ w3 + b3)

        def _twist(x):
            o_r, o_i, p_r, p_i = jnp.split(x, 4, axis=-1)
            return jnp.concatenate([p_r, -p_i, -o_r, o_i], axis=-1)
        key = jax.random.key(seed)
        ks = jax.random.split(key, 9)
        d = DIM

        def w(k, fan_in, fan_out):
            return jax.random.normal(k, (fan_in, fan_out), dtype=jnp.float32) / np.sqrt(fan_in).astype(np.float32)
        inp = {'x': jax.random.normal(ks[0], (B, S, d), dtype=jnp.float32)}
        cn_dims = [(d, d), (d, d // 2), (d // 2, d // 4), (d // 4, 1)]
        for i, (a, b) in enumerate(cn_dims):
            inp[f'cn_w{i + 1}'] = w(ks[1 + i], a, b)
            inp[f'cn_b{i + 1}'] = jnp.zeros((b,), dtype=jnp.float32)
        gc_dims = [(d, d // 2), (d // 2, d // 4), (d // 4, 1)]
        for i, (a, b) in enumerate(gc_dims):
            inp[f'gc_w{i + 1}'] = w(ks[5 + i], a, b)
            inp[f'gc_b{i + 1}'] = jnp.zeros((b,), dtype=jnp.float32)
        inp['adaptive_range'] = jnp.full((1,), 0.2, dtype=jnp.float32)
        return inp
    _L0_ffn_in = _L0_ffn_setup()
    _L0_c = _w((lambda *s: np.random.randn(*s).astype(np.float32) * 0.05)(4, 128))
    _L0_wmod = _w((lambda *s: np.random.randn(*s).astype(np.float32) * 0.05)(128, 6 * 128) * 128 ** (-0.5))

    def _L1_attn_setup():
        import jax, jax.numpy as jnp
        import numpy as np
        WINDOW = 64
        SHIFT = 32
        HEADS = 8
        key = jax.random.key(seed)
        k1, k2, k3 = jax.random.split(key, 3)
        B, L, D = (8, 512, 128)
        scale = 0.02
        return {'x': jax.random.normal(k1, (B, L, D), dtype=jnp.float32), 'in_proj_w': jax.random.normal(k2, (3 * D, D), dtype=jnp.float32) * scale, 'in_proj_b': jnp.zeros((3 * D,), dtype=jnp.float32), 'out_w': jax.random.normal(k3, (D, D), dtype=jnp.float32) * scale, 'out_b': jnp.zeros((D,), dtype=jnp.float32)}
    _L1_attn_in = _L1_attn_setup()

    def _L1_ffn_setup():
        import math
        import jax, jax.numpy as jnp
        import numpy as np
        B, S, D, H, E, K = (4, 256, 128, 512, 8, 2)
        CAPACITY_RATIO = 1.05
        key = jax.random.key(seed)
        k0, k1, k2, k3 = jax.random.split(key, 4)
        x = jax.random.normal(k0, (B, S, D), jnp.float32)
        Wg = jax.random.normal(k1, (D, E), jnp.float32) * 0.02
        W1 = jax.random.normal(k2, (E, D, H), jnp.float32) * 0.02
        b1 = jnp.zeros((E, H), jnp.float32)
        W2 = jax.random.normal(k3, (E, H, D), jnp.float32) * 0.02
        b2 = jnp.zeros((E, D), jnp.float32)
        return {'x': x, 'Wg': Wg, 'W1': W1, 'b1': b1, 'W2': W2, 'b2': b2}
    _L1_ffn_in = _L1_ffn_setup()
    _L1_c = _w((lambda *s: np.random.randn(*s).astype(np.float32) * 0.05)(4, 128))
    _L1_wmod = _w((lambda *s: np.random.randn(*s).astype(np.float32) * 0.05)(128, 6 * 128) * 128 ** (-0.5))
    _d = {'L0_attn_x': _L0_attn_in['x'], 'L0_attn_Wq': _L0_attn_in['Wq'], 'L0_attn_bq': _L0_attn_in['bq'], 'L0_attn_Wk': _L0_attn_in['Wk'], 'L0_attn_bk': _L0_attn_in['bk'], 'L0_attn_Wv': _L0_attn_in['Wv'], 'L0_attn_bv': _L0_attn_in['bv'], 'L0_attn_Wo': _L0_attn_in['Wo'], 'L0_attn_bo': _L0_attn_in['bo'], 'L0_ffn_cn_w1': _L0_ffn_in['cn_w1'], 'L0_ffn_cn_b1': _L0_ffn_in['cn_b1'], 'L0_ffn_cn_w2': _L0_ffn_in['cn_w2'], 'L0_ffn_cn_b2': _L0_ffn_in['cn_b2'], 'L0_ffn_cn_w3': _L0_ffn_in['cn_w3'], 'L0_ffn_cn_b3': _L0_ffn_in['cn_b3'], 'L0_ffn_cn_w4': _L0_ffn_in['cn_w4'], 'L0_ffn_cn_b4': _L0_ffn_in['cn_b4'], 'L0_ffn_gc_w1': _L0_ffn_in['gc_w1'], 'L0_ffn_gc_b1': _L0_ffn_in['gc_b1'], 'L0_ffn_gc_w2': _L0_ffn_in['gc_w2'], 'L0_ffn_gc_b2': _L0_ffn_in['gc_b2'], 'L0_ffn_gc_w3': _L0_ffn_in['gc_w3'], 'L0_ffn_gc_b3': _L0_ffn_in['gc_b3'], 'L0_ffn_adaptive_range': _L0_ffn_in['adaptive_range'], 'L0_c': _L0_c, 'L0_wmod': _L0_wmod, 'L1_attn_in_proj_w': _L1_attn_in['in_proj_w'], 'L1_attn_in_proj_b': _L1_attn_in['in_proj_b'], 'L1_attn_out_w': _L1_attn_in['out_w'], 'L1_attn_out_b': _L1_attn_in['out_b'], 'L1_ffn_Wg': _L1_ffn_in['Wg'], 'L1_ffn_W1': _L1_ffn_in['W1'], 'L1_ffn_b1': _L1_ffn_in['b1'], 'L1_ffn_W2': _L1_ffn_in['W2'], 'L1_ffn_b2': _L1_ffn_in['b2'], 'L1_c': _L1_c, 'L1_wmod': _L1_wmod}
    _x0 = _d['L0_attn_x']
    _d['L0_attn_x'] = jax.random.normal(jax.random.fold_in(jax.random.key(seed), 1), (4, 1024, 128), dtype=_x0.dtype)
    del _x0
    return _d

def reference(L0_attn_x, L0_attn_Wq, L0_attn_bq, L0_attn_Wk, L0_attn_bk, L0_attn_Wv, L0_attn_bv, L0_attn_Wo, L0_attn_bo, L0_ffn_cn_w1, L0_ffn_cn_b1, L0_ffn_cn_w2, L0_ffn_cn_b2, L0_ffn_cn_w3, L0_ffn_cn_b3, L0_ffn_cn_w4, L0_ffn_cn_b4, L0_ffn_gc_w1, L0_ffn_gc_b1, L0_ffn_gc_w2, L0_ffn_gc_b2, L0_ffn_gc_w3, L0_ffn_gc_b3, L0_ffn_adaptive_range, L0_c, L0_wmod, L1_attn_in_proj_w, L1_attn_in_proj_b, L1_attn_out_w, L1_attn_out_b, L1_ffn_Wg, L1_ffn_W1, L1_ffn_b1, L1_ffn_W2, L1_ffn_b2, L1_c, L1_wmod):

    def _L0_attn_ref(x, Wq, bq, Wk, bk, Wv, bv, Wo, bo):
        import jax, jax.numpy as jnp
        import numpy as np
        D_MODEL, H, DK, DV = (128, 16, 64, 64)
        B, S, _ = x.shape
        q = (x @ Wq + bq).reshape(B, S, H, DK)
        k = x @ Wk + bk
        v = x @ Wv + bv
        scores = jnp.einsum('bshd,btd->bhst', q, k) / np.sqrt(DK).astype(x.dtype)
        w = jax.nn.softmax(scores, axis=-1)
        out = jnp.einsum('bhst,btd->bshd', w, v).reshape(B, S, H * DV)
        return out @ Wo + bo

    def _L0_ffn_ref(x, cn_w1, cn_b1, cn_w2, cn_b2, cn_w3, cn_b3, cn_w4, cn_b4, gc_w1, gc_b1, gc_w2, gc_b2, gc_w3, gc_b3, adaptive_range):
        import jax, jax.numpy as jnp
        import numpy as np
        B, S, DIM = (4, 512, 128)
        BASE_COUPLING = 0.1
        NUM_CYCLES = 3

        def _gelu(x):
            return jax.nn.gelu(x, approximate=False)

        def _coupling_net(h, w1, b1, w2, b2, w3, b3, w4, b4):
            h = _gelu(h @ w1 + b1)
            h = _gelu(h @ w2 + b2)
            h = _gelu(h @ w3 + b3)
            return jax.nn.sigmoid(h @ w4 + b4)

        def _global_net(h, w1, b1, w2, b2, w3, b3):
            h = _gelu(h @ w1 + b1)
            h = _gelu(h @ w2 + b2)
            return jax.nn.sigmoid(h @ w3 + b3)

        def _twist(x):
            o_r, o_i, p_r, p_i = jnp.split(x, 4, axis=-1)
            return jnp.concatenate([p_r, -p_i, -o_r, o_i], axis=-1)
        global_context = x.mean(axis=1, keepdims=True)
        gf = _global_net(global_context, gc_w1, gc_b1, gc_w2, gc_b2, gc_w3, gc_b3)
        out = x
        for _ in range(NUM_CYCLES):
            tf = _coupling_net(out, cn_w1, cn_b1, cn_w2, cn_b2, cn_w3, cn_b3, cn_w4, cn_b4)
            combined = 0.7 * gf + 0.3 * tf
            coupling = BASE_COUPLING + adaptive_range * (combined - 0.5) * 2.0
            out = out + coupling * _twist(out)
        return out

    def _L1_attn_ref(x, in_proj_w, in_proj_b, out_w, out_b):
        import jax, jax.numpy as jnp
        import numpy as np
        WINDOW = 64
        SHIFT = 32
        HEADS = 8
        B, L, D = x.shape
        H, W, S = (HEADS, WINDOW, SHIFT)
        hd = D // H
        xs = jnp.roll(x, -S, axis=1)
        nw = L // W
        xw = xs.reshape(B * nw, W, D)
        qkv = xw @ in_proj_w.T + in_proj_b
        q, k, v = jnp.split(qkv, 3, axis=-1)

        def to_heads(t):
            return t.reshape(-1, W, H, hd).transpose(0, 2, 1, 3)
        q, k, v = (to_heads(q), to_heads(k), to_heads(v))
        scores = jnp.einsum('nhqd,nhkd->nhqk', q, k) * (1.0 / np.sqrt(hd))
        attn = jax.nn.softmax(scores, axis=-1)
        o = jnp.einsum('nhqk,nhkd->nhqd', attn, v)
        o = o.transpose(0, 2, 1, 3).reshape(-1, W, D)
        o = o @ out_w.T + out_b
        o = o.reshape(B, L, D)
        o = jnp.roll(o, S, axis=1)
        return o + o

    def _L1_ffn_ref(x, Wg, W1, b1, W2, b2):
        import math
        import jax, jax.numpy as jnp
        import numpy as np
        B, S, D, H, E, K = (4, 256, 128, 512, 8, 2)
        CAPACITY_RATIO = 1.05
        b, s, d = x.shape
        e = Wg.shape[1]
        n = b * s
        cap = int(math.ceil(n * K / e * CAPACITY_RATIO))
        xf = x.reshape(n, d)
        probs = jax.nn.softmax(xf @ Wg, axis=-1)
        topv, topi = jax.lax.top_k(probs, K)
        gates = topv / jnp.sum(topv, axis=-1, keepdims=True)
        eidx = topi.reshape(-1)
        oh = jax.nn.one_hot(eidx, e, dtype=jnp.int32)
        pos = jnp.sum(jnp.cumsum(oh, axis=0) * oh, axis=-1) - 1
        keep = pos < cap
        dest = jnp.where(keep, eidx * cap + pos, e * cap)
        xr = jnp.repeat(xf, K, axis=0)
        buf = jnp.zeros((e * cap + 1, d), x.dtype).at[dest].set(xr)
        expert_in = buf[:e * cap].reshape(e, cap, d)
        h = jax.nn.gelu(jnp.einsum('ecd,edh->ech', expert_in, W1) + b1[:, None, :])
        y = jnp.einsum('ech,ehd->ecd', h, W2) + b2[:, None, :]
        yf = jnp.concatenate([y.reshape(e * cap, d), jnp.zeros((1, d), y.dtype)], axis=0)
        gathered = yf[dest]
        w = (gates.reshape(-1) * keep.astype(gates.dtype))[:, None]
        out = (gathered * w).reshape(n, K, d).sum(axis=1).reshape(b, s, d)
        return out
    x = L0_attn_x
    mod = (_silu(L0_c) @ L0_wmod).reshape(L0_c.shape[0], 6, 1, -1)
    sa, ca, ga, sb, cb, gb = (mod[:, 0], mod[:, 1], mod[:, 2], mod[:, 3], mod[:, 4], mod[:, 5])
    ga = (2 * (ga >= 0) - 1) * jnp.maximum(jnp.abs(ga), 0.25)
    gb = (2 * (gb >= 0) - 1) * jnp.maximum(jnp.abs(gb), 0.25)
    h = _layernorm(x, axis=-1) * (1 + ca) + sa
    x = x + ga * _L0_attn_ref(h, L0_attn_Wq, L0_attn_bq, L0_attn_Wk, L0_attn_bk, L0_attn_Wv, L0_attn_bv, L0_attn_Wo, L0_attn_bo)
    h = _layernorm(x, axis=-1) * (1 + cb) + sb
    x = x + gb * _L0_ffn_ref(h, L0_ffn_cn_w1, L0_ffn_cn_b1, L0_ffn_cn_w2, L0_ffn_cn_b2, L0_ffn_cn_w3, L0_ffn_cn_b3, L0_ffn_cn_w4, L0_ffn_cn_b4, L0_ffn_gc_w1, L0_ffn_gc_b1, L0_ffn_gc_w2, L0_ffn_gc_b2, L0_ffn_gc_w3, L0_ffn_gc_b3, L0_ffn_adaptive_range)
    mod = (_silu(L1_c) @ L1_wmod).reshape(L1_c.shape[0], 6, 1, -1)
    sa, ca, ga, sb, cb, gb = (mod[:, 0], mod[:, 1], mod[:, 2], mod[:, 3], mod[:, 4], mod[:, 5])
    ga = (2 * (ga >= 0) - 1) * jnp.maximum(jnp.abs(ga), 0.25)
    gb = (2 * (gb >= 0) - 1) * jnp.maximum(jnp.abs(gb), 0.25)
    h = _layernorm(x, axis=-1) * (1 + ca) + sa
    x = x + ga * _L1_attn_ref(h, L1_attn_in_proj_w, L1_attn_in_proj_b, L1_attn_out_w, L1_attn_out_b)
    h = _layernorm(x, axis=-1) * (1 + cb) + sb
    x = x + gb * _L1_ffn_ref(h, L1_ffn_Wg, L1_ffn_W1, L1_ffn_b1, L1_ffn_W2, L1_ffn_b2)
    return x

_drawn_inputs = setup_inputs


def setup_inputs(seed=0):
    import zlib

    import numpy as np

    out = dict(_drawn_inputs(seed))
    spreads = {'L0_ffn_cn_b1': (0.0, 2.0),
     'L0_ffn_cn_b2': (0.0, 2.0),
     'L0_ffn_cn_b3': (0.0, 2.0),
     'L0_ffn_gc_b1': (0.0, 2.0),
     'L0_ffn_gc_b2': (0.0, 2.0),
     'L1_attn_in_proj_b': (0.0, 0.753),
     'L1_attn_out_b': (0.0, 0.418),
     'L1_ffn_b1': (0.0, 0.8),
     'L1_ffn_b2': (0.0, 1.59)}
    factors = {'L0_attn_Wq': 8.0,
     'L0_attn_bq': 8.0,
     'L0_attn_Wk': 8.0,
     'L0_attn_bk': 200.0,
     'L0_attn_Wv': 8.0,
     'L0_attn_bv': 6.165,
     'L0_attn_Wo': 5.532,
     'L0_attn_bo': 28.846,
     'L0_ffn_cn_w1': 80.345,
     'L0_ffn_cn_w2': 85.763,
     'L0_ffn_cn_w3': 78.669,
     'L0_ffn_cn_w4': 84.224,
     'L0_ffn_gc_w1': 8.0,
     'L0_ffn_gc_w2': 8.0,
     'L0_ffn_gc_w3': 8.0,
     'L1_attn_in_proj_w': 8.0,
     'L1_attn_out_w': 5.139,
     'L1_ffn_Wg': 3.109,
     'L1_ffn_W1': 6.159,
     'L1_ffn_W2': 5.565}
    for name, (base, spread) in spreads.items():
        noise = np.random.default_rng([zlib.crc32(name.encode()), seed]).standard_normal(out[name].shape)
        drawn = base * np.exp(spread * noise) if base else spread * noise
        out[name] = jnp.asarray(drawn.astype(out[name].dtype))
    for name, factor in factors.items():
        out[name] = (out[name] * factor).astype(out[name].dtype)
    return out
```

```python
import math
from contextlib import ExitStack

import numpy as np

import concourse.bass as bass
from concourse import mybir

F32 = mybir.dt.float32
F32R = mybir.dt.float32r
BF16 = mybir.dt.bfloat16
ALU = mybir.AluOpType
ACT = mybir.ActivationFunctionType
AX = mybir.AxisListType

P = 128
B, S = 4, 1024
N = B * S
TILE = 512
NT = N // TILE
H, DK = 16, 64
SB = 128
NB = N // SB
BPB = S // SB
KC = S // P
EPS = 1e-5
W, HEADS, HD, SHIFT = 64, 8, 16, 32
E, HID, TOPK = 8, 512, 2
CAP = math.ceil(N * TOPK / E * 1.05)
HC = HID // P
BIG = 1.0e30


class Chain:

    def __init__(self, sem):
        self.sem, self.n = sem, 0

    def inc(self, ins, by=1):
        self.n += by
        ins.then_inc(self.sem, by)
        return self.n


class Program:
    def __init__(self, nc, a, out):
        self.nc, self.a, self.out = nc, a, out
        self.ctx = ExitStack()
        self.names = 0

    def sem(self, name):
        return self.ctx.enter_context(self.nc.semaphore(name))

    def sb(self, ctx, name, shape, dt=F32):
        return ctx.enter_context(self.nc.sbuf_tensor(name, shape, dt))


def build(nc, a, out, stop=99, only=0):
    prog = Program(nc, a, out)
    with prog.ctx as ctx:
        sb = lambda name, shape, dt=F32: prog.sb(ctx, name, shape, dt)
        pairs = [ctx.enter_context(nc.psum_tensor(f"pair{i}", [P, 2 * TILE], F32)) for i in range(4)]
        banks = [pairs[3][:, i * TILE:(i + 1) * TILE] for i in range(2)]
        prog.banks, prog.pairs = banks, pairs
        prog.x = sb("x", [P, N])
        prog.mean_w = sb("mean_w", [P, P])
        prog.ones = sb("ones", [P, P])
        prog.ident = sb("ident", [P, P])
        prog.mods = sb("mods", [P, 2, 6, B])
        prog.zero_col = sb("zero_col", [P, 1])
        prog.eps_col = sb("eps_col", [P, 1])
        prog.done = prog.sem("phase_done")
        prog.phases = 0
        setup(prog)
        if stop >= 1 and only in (0, 1):
            attention0(prog)
        if stop >= 2 and only in (0, 2):
            twist_net(prog)
        if stop >= 3 and only in (0, 3):
            attention1(prog)
        if stop >= 4 and only in (0, 4):
            experts(prog)
        store(prog)


def phase(prog, parts):
    nc = prog.nc
    prog.phases += 1
    total = 5 * prog.phases
    with nc.Block() as block:
        engines = dict(sync=block.sync, gpsimd=block.gpsimd, scalar=block.scalar, vector=block.vector,
                       tensor=block.tensor)
        for name, on_engine in engines.items():
            part = parts.get(name)

            def body(eng, part=part):
                if part:
                    part(eng)
                eng.sem_inc(prog.done, 1)
                eng.wait_ge(prog.done, total)
            on_engine(body)


def setup(prog):
    nc, a = prog.nc, prog.a
    with ExitStack() as ctx:
        sb = lambda name, shape, dt=F32: prog.sb(ctx, name, shape, dt)
        wmod = sb("wmod", [P, 2, 6 * P])
        ct = sb("ct", [P, 2 * B])
        den = sb("den", [P, 2 * B])
        sig = sb("sig", [P, 2 * B])
        act = sb("act", [P, 2 * B])
        sgn = sb("sgn", [P, 2, 2, B])
        mag = sb("mag", [P, 2, 2, B])
        loaded, x_in = prog.sem("mod_loaded"), prog.sem("x_in")
        s_id, s_v, s_a, s_p = (prog.sem(n) for n in ("ident_made", "mod_v", "mod_a", "mod_p"))
        ps = prog.banks[0]
        mods = prog.mods

        def sync(e):
            for l in range(2):
                e.dma_start(wmod[:, l, :], a[f"L{l}_wmod"]).then_inc(loaded, 16)
                e.dma_start(ct[:, l * B:(l + 1) * B], a[f"L{l}_c"]).then_inc(loaded, 16)
            for t in range(NT):
                e.dma_start(prog.x[:, t * TILE:(t + 1) * TILE], a["x"][:, t * TILE:(t + 1) * TILE]).then_inc(x_in, 16)
            e.wait_ge(x_in, 16 * NT)

        def gpsimd(e):
            e.memset(prog.ident[:, :], 0.0).then_inc(s_id, 1)
            e.wait_ge(s_id, 1)
            e.affine_select(out=prog.ident[:, :], in_=prog.ident[:, :], compare_op=ALU.not_equal, fill=1.0,
                            base=0, pattern=[[-1, P]], channel_multiplier=1).then_inc(s_id, 1)
            e.memset(prog.mean_w[:, :], 1.0 / P)
            e.memset(prog.ones[:, :], 1.0)
            e.memset(prog.zero_col[:, :], 0.0)
            e.memset(prog.eps_col[:, :], EPS).then_inc(s_id, 1)
            e.wait_ge(s_id, 3)

        def scalar(e):
            e.wait_ge(loaded, 64)
            e.activation(den[:, :], ct[:, :], ACT.Exp, scale=-1.0).then_inc(s_a, 1)

        def vector(e):
            v = Chain(s_v)
            step = lambda ins: e.wait_ge(s_v, v.inc(ins))
            e.wait_ge(s_a, 1)
            step(e.tensor_scalar(den[:, :], den[:, :], 1.0, None, ALU.add))
            step(e.reciprocal(sig[:, :], den[:, :]))
            v.inc(e.tensor_tensor(act[:, :], ct[:, :], sig[:, :], ALU.mult))
            e.wait_ge(s_p, 1)
            got = ps[:, 0:2 * 6 * B].rearrange("p (l k b) -> p l k b", l=2, k=6)
            step(e.tensor_copy(mods[:, :, :, :], got))
            for l in range(2):
                for j in range(2):
                    sc, g = mods[:, l, 3 * j + 1, :], mods[:, l, 3 * j + 2, :]
                    s_, m_ = sgn[:, l, j, :], mag[:, l, j, :]
                    step(e.tensor_scalar(sc, sc, 1.0, None, ALU.add))
                    step(e.tensor_scalar(s_, g, 0.0, 2.0, ALU.is_ge, ALU.mult))
                    step(e.tensor_scalar(s_, s_, -1.0, None, ALU.add))
                    step(e.tensor_tensor(m_, s_, g, ALU.mult))
                    step(e.tensor_scalar(m_, m_, 0.25, None, ALU.max))
                    step(e.tensor_tensor(g, s_, m_, ALU.mult))

        def tensor(e):
            e.wait_ge(s_v, 3)
            for l in range(2):
                for k in range(6):
                    o = (l * 6 + k) * B
                    last = e.matmul(ps[:, o:o + B], wmod[:, l, k * P:(k + 1) * P], act[:, l * B:(l + 1) * B],
                                    start=True, stop=True)
            last.then_inc(s_p, 1)

        phase(prog, dict(sync=sync, gpsimd=gpsimd, scalar=scalar, vector=vector, tensor=tensor))


def store(prog):
    s = prog.sem("stored")

    def sync(e):
        for t in range(NT):
            sl = slice(t * TILE, (t + 1) * TILE)
            e.dma_start(prog.out[:, sl], prog.x[:, sl]).then_inc(s, 16)
        e.wait_ge(s, 16 * NT)
    phase(prog, dict(sync=sync))


class Norm:

    def __init__(self, prog, ctx, tag, layer, j):
        self.prog, self.layer, self.j = prog, layer, j
        sb = lambda name, shape, dt=F32: prog.sb(ctx, f"{tag}_{name}", shape, dt)
        self.xc = sb("xc", [P, 2, TILE])
        self.sq = sb("sq", [P, 2, TILE])
        self.xn = sb("xn", [P, 2, TILE])
        s = lambda n: prog.sem(f"{tag}_{n}")
        self.s_mean, self.s_xc, self.s_sq, self.s_var, self.s_rstd, self.s_xn = (
            s(n) for n in ("mean", "xc", "sq", "var", "rstd", "xn"))
        self.s_ln = s("ln")
        self.mean_ps, self.var_ps = prog.pairs[0], prog.pairs[1]

    def tensor(self, e, b):
        x, w = self.prog.x, self.prog.mean_w
        for t in range(2):
            e.matmul(self.mean_ps[:, t * TILE:(t + 1) * TILE], w[:, :], x[:, bass.ds(b * S + t * TILE, TILE)],
                     start=True, stop=True).then_inc(self.s_mean, 1)
        for t in range(2):
            e.wait_ge(self.s_sq, 2 * b + t + 1)
            e.matmul(self.var_ps[:, t * TILE:(t + 1) * TILE], w[:, :], self.sq[:, t, :],
                     start=True, stop=True).then_inc(self.s_var, 1)

    def vector(self, e, b):
        x = self.prog.x
        for t in range(2):
            e.wait_ge(self.s_mean, 2 * b + t + 1)
            e.tensor_tensor(self.xc[:, t, :], x[:, bass.ds(b * S + t * TILE, TILE)],
                            self.mean_ps[:, t * TILE:(t + 1) * TILE], ALU.subtract).then_inc(self.s_xc, 1)
        for t in range(2):
            e.wait_ge(self.s_rstd, 2 * b + t + 1)
            e.tensor_tensor(self.xn[:, t, :], self.xc[:, t, :], self.sq[:, t, :],
                            ALU.mult).then_inc(self.s_xn, 1)
        e.wait_ge(self.s_xn, 2 * b + 2)

    @staticmethod
    def tables(e):
        e.preload_act_table_set("natural_log_exp_and_others")

    def scalar(self, e, b):
        for t in range(2):
            e.wait_ge(self.s_xc, 2 * b + t + 1)
            e.activation(self.sq[:, t, :], self.xc[:, t, :], ACT.Square).then_inc(self.s_sq, 1)
        for t in range(2):
            e.wait_ge(self.s_var, 2 * b + t + 1)
            e.activation(self.sq[:, t, :], self.var_ps[:, t * TILE:(t + 1) * TILE], ACT.Ln,
                         bias=self.prog.eps_col[:, 0:1]).then_inc(self.s_ln, 1)
        for t in range(2):
            e.wait_ge(self.s_ln, 2 * b + t + 1)
            e.activation(self.sq[:, t, :], self.sq[:, t, :], ACT.Exp, scale=-0.5).then_inc(self.s_rstd, 1)

    def affine(self, e, b, t, dst, cols=(0, TILE), accum=None):
        m = self.prog.mods
        e.wait_ge(self.prog.done, 5)
        e.wait_ge(self.s_xn, 2 * b + t + 1)
        return e.activation(dst, self.xn[:, t, cols[0]:cols[1]], ACT.Identity,
                            scale=m[:, self.layer, 3 * self.j + 1, bass.ds(b, 1)],
                            bias=m[:, self.layer, 3 * self.j, bass.ds(b, 1)],
                            **({"accum_out": accum} if accum is not None else {}))


def attention0(prog):
    with ExitStack() as ctx:
        sb = lambda name, shape, dt=F32: prog.sb(ctx, name, shape, dt)
        t = dict(
            hT=sb("hT", [P, N + SB]),
            wq=sb("wq", [P, H * DK]), wo=sb("wo", [P, H * DK // P, P]),
            wk=sb("wk", [P, 2 * DK]), wv=sb("wv", [P, DK]),
            bq=sb("bq", [P, H * DK // P]), bk=sb("bk", [P, 1]), bv=sb("bv", [P, DK]), bo=sb("bo", [P, 1]),
            khi_all=sb("khi_all", [P, N + S], F32R), klo_all=sb("klo_all", [P, N], F32R),
            v_all=sb("v_all", [P, B * KC * DK]),
        )
        k_and_v(prog, ctx, t)
        scores_and_values(prog, ctx, t)


def k_and_v(prog, octx, t):
    a = prog.a
    hT, khi_all, klo_all, v_all = t["hT"], t["khi_all"], t["klo_all"], t["v_all"]
    with ExitStack() as ctx:
        norm = Norm(prog, ctx, "ln0", 0, 0)
        hfix = prog.sb(ctx, "hfix", [P, 2, TILE])
        s_w, s_w2, s_h, s_hf, s_k, s_khi, s_klo, s_v, s_ve, s_z = (prog.sem(f"kv_{n}") for n in (
            "w", "wlate", "h", "hfix", "k", "khi", "klo", "v", "v_out", "zeros"))
        kps, vps = prog.pairs[2], prog.banks[0]

        def sync(e):
            for c in range(2):
                e.dma_start(t["wk"][:, c * DK:(c + 1) * DK], a["L0_attn_Wk"]).then_inc(s_w, 16)
                e.dma_start(t["bk"][c * DK:(c + 1) * DK, :], a["L0_attn_bk"].unsqueeze(1)).then_inc(s_w, 16)
            e.dma_start(t["wv"][:, :], a["L0_attn_Wv"]).then_inc(s_w, 16)
            e.dma_start(t["bv"][:, :], a["L0_attn_bv"].partition_broadcast(P)).then_inc(s_w, 16)
            e.dma_start(t["wq"][:, :], a["L0_attn_Wq"]).then_inc(s_w2, 16)
            e.dma_start(t["bq"][:, :], a["L0_attn_bq"]).then_inc(s_w2, 16)
            e.dma_start(t["wo"][:, :, :], a["L0_attn_Wo"].rearrange("(j p) n -> p j n", p=P)).then_inc(s_w2, 16)
            e.dma_start(t["bo"][:, :], a["L0_attn_bo"].unsqueeze(1)).then_inc(s_w2, 16)
            e.wait_ge(s_w2, 64)

        def gpsimd(e):
            e.memset(hT[:, N:N + SB], 0.0).then_inc(s_z, 1)
            e.memset(khi_all[:, N:N + S].bitcast(F32), 0.0).then_inc(s_z, 1)
            e.wait_ge(s_z, 2)

        def scalar(e):
            norm.tables(e)
            with e.Fori(0, B) as b:
                norm.scalar(e, b)
                for c in range(2):
                    norm.affine(e, b, c, hT[:, bass.ds(b * S + c * TILE, TILE)]).then_inc(s_h, 1)
                    norm.affine(e, b, c, hfix[:, c, :]).then_inc(s_hf, 1)
                for c in range(2):
                    e.wait_ge(s_w, 96)
                    e.wait_ge(s_k, 2 * b + c + 1)
                    sl = bass.ds(b * S + c * TILE, TILE)
                    e.activation(khi_all[:, sl], kps[:, c * TILE:(c + 1) * TILE], ACT.Identity,
                                 bias=t["bk"][:, 0:1]).then_inc(s_khi, 1)

        def vector(e):
            with e.Fori(0, B) as b:
                norm.vector(e, b)
                for c in range(2):
                    sl = bass.ds(b * S + c * TILE, TILE)
                    e.wait_ge(s_khi, 2 * b + c + 1)
                    e.scalar_tensor_tensor(out=klo_all[:, sl], in0=kps[:, c * TILE:(c + 1) * TILE],
                                           scalar=t["bk"][:, 0:1], in1=khi_all[:, sl], op0=ALU.add,
                                           op1=ALU.subtract).then_inc(s_klo, 1)
                e.wait_ge(s_v, b + 1)
                o = v_all[:, bass.ds(b * KC * DK, KC * DK)].rearrange("p (c d) -> p c d", d=DK)
                e.tensor_tensor(o, vps[:, :].rearrange("p (c d) -> p c d", d=DK),
                                t["bv"][:, :].unsqueeze(1).to_broadcast([P, KC, DK]), ALU.add).then_inc(s_ve, 1)

        def tensor(e):
            with e.Fori(0, B) as b:
                norm.tensor(e, b)
                e.wait_ge(s_w, 96)
                for c in range(2):
                    e.wait_ge(s_hf, 2 * b + c + 1)
                    e.matmul(kps[:, c * TILE:(c + 1) * TILE], t["wk"][:, :], hfix[:, c, :],
                             start=True, stop=True).then_inc(s_k, 1)
                for c in range(KC):
                    last = e.matmul(vps[:, c * DK:(c + 1) * DK],
                                    hfix[:, c // 4, (c % 4) * P:(c % 4 + 1) * P], t["wv"][:, :],
                                    start=True, stop=True)
                last.then_inc(s_v, 1)
                e.wait_ge(s_klo, 2 * b + 2)
                e.wait_ge(s_ve, b + 1)

        phase(prog, dict(sync=sync, gpsimd=gpsimd, scalar=scalar, vector=vector, tensor=tensor))


def scores_and_values(prog, ctx, t):
    hT, khi_all, klo_all, v_all = t["hT"], t["khi_all"], t["klo_all"], t["v_all"]
    wq, wo, bq, bo, x, mods = t["wq"], t["wo"], t["bq"], t["bo"], prog.x, prog.mods
    sb = lambda name, shape, dt=F32: prog.sb(ctx, name, shape, dt)
    HALF, SET = DK, 4 * SB
    NP = 8
    khi = sb("khi", [P, S], F32R)
    klo = [sb(f"klo{r}", [P, S], F32R) for r in range(2)]
    v = sb("v", [P, KC * DK])
    q1 = [sb(f"q1_{i}", [P, 4 * SET], F32R) for i in range(2)]
    q2 = [sb(f"q2_{i}", [P, 4 * SET], F32R) for i in range(2)]
    qf = sb("qf", [P, SET])
    pr = [sb(f"p{i}", [P, 2 * SET]) for i in range(NP)]
    part = sb("part", [P, 2 * SET])
    total = sb("total", [P, 2 * SET])
    osb = sb("osb", [P, SET])
    inv = sb("inv", [P, SET])
    on = sb("on", [P, 2 * SET])
    mx = sb("mx", [P, 2, H])
    mrow = sb("mrow", [P, H])
    mneg = sb("mneg", [H, SB], F32R)
    y = sb("y", [P, SB])

    s = lambda n: prog.sem(f"a0_{n}")
    BIAS = 16
    st, ex, pv = s("scores"), s("exps"), s("pv")
    qp, qs, qhi, q2s, qlo = s("q"), s("q_biased"), s("q_hi"), s("q_hi2"), s("q_lo")
    ms, mr = s("row_scores"), s("row_max")
    mc, mt, mn, md = s("max"), s("max_T"), s("max_neg"), s("max_row")
    pa, da = s("part_sum"), s("total_sum")
    ls, lg, rc, oe, od = s("sum_all"), s("sum_ln"), s("inverse"), s("pv_out"), s("normed")
    ys, yb, xs = s("y"), s("y_biased"), s("x_done")
    kc = s("k_copied")
    zs = s("rows_zeroed")
    bank = [prog.pairs[0], prog.pairs[1]]
    row, (obank, misc) = prog.pairs[2], prog.banks
    chunk = lambda ap, c: ap[:, c * P:(c + 1) * P]

    def at(g, per, k):
        return g * per + (BIAS + k)

    MAXSTEPS = {3: 4, 4: 4, 5: 4, 6: 4, 7: 4, 8: 3, 9: 3, 10: 3, 11: 3}
    starts, n0 = {}, 0
    for k_, m_ in MAXSTEPS.items():
        starts[k_] = (n0, n0 + m_)
        n0 += m_
    assert n0 == 2 * H

    def head_cols(h):
        u, slot, par = h // 8, (h % 8) // 2, h % 2
        return ((2 * par + u) * 4 + slot) * SB

    class TensorSide:
        def __init__(self, e):
            self.e = e

        def project_q(self, n, u):
            e = self.e
            for slot in range(4):
                j = 4 * u + slot
                last = e.matmul(misc[:, slot * SB:(slot + 1) * SB], wq[:, j * P:(j + 1) * P],
                                hT[:, bass.ds(n * SB, SB)], start=True, stop=True)
            last.then_inc(qp, 1)

        def row_scores(self, n, nb, p, j):
            e, h, half = self.e, j // 2, j % 2
            if j % 16 == 0:
                e.wait_ge(qlo, at(n, 2, j // 16 + 1))
            e.wait_ge(mr, at(n, 32, j - 1))
            c = head_cols(h)
            e.matmul(row[:, half * TILE:(half + 1) * TILE], q1[p][:, c:c + SB],
                     khi_all[:, bass.ds(nb * S + half * TILE, TILE)], start=True, stop=True).then_inc(ms, 1)

        def turn_max(self, n):
            e = self.e
            e.wait_ge(mc, at(n, 1, 1))
            e.matmul(misc[0:H, 0:SB], mrow[:, :], prog.ident[:, :], is_transpose=True).then_inc(mt, 1)

        def scores(self, g, p, k):
            e, u, c = self.e, k // 8, k % 8
            e.wait_ge(ex, at(g, 16, k - 1))
            if k == 0:
                e.wait_ge(md, at(g, 32, 32))
                e.wait_ge(q2s, at(g, 2, 2))
            ps = bank[k % 2]
            for par in range(2):
                e.matmul(ps[:, par * SET:(par + 1) * SET], chunk(khi, c),
                         q1[p][:, (2 * par + u) * SET:(2 * par + u + 1) * SET], start=True, stop=False)
            for par in range(2):
                last = e.matmul(ps[:, par * SET:(par + 1) * SET], chunk(klo[par], c),
                                q2[p][:, (2 * par + u) * SET:(2 * par + u + 1) * SET], start=False, stop=True)
            last.then_inc(st, 1)

        def values(self, g, k):
            e, c = self.e, k % 8
            e.wait_ge(ex, at(g, 16, k + 1))
            if c == 0:
                e.wait_ge(oe, at(g, 2, k // 8))
            for par in range(2):
                last = e.matmul(obank[par * HALF:(par + 1) * HALF, :], v[:, c * DK:(c + 1) * DK],
                                pr[k % NP][:, par * SET:(par + 1) * SET], start=(c == 0), stop=(c == KC - 1))
            last.then_inc(pv, 1)

        def sums(self, g, u):
            e = self.e
            e.wait_ge(da, at(g, 4, 2 * u + 2))
            for par in range(2):
                last = e.matmul(misc[par * HALF:(par + 1) * HALF, :], prog.ones[:, 0:HALF],
                                total[:, par * SET:(par + 1) * SET], start=True, stop=True)
            last.then_inc(ls, 1)

        def project_out(self, g):
            e = self.e
            e.wait_ge(od, at(g, 2, 2))
            for j in range(H // 2):
                last = e.matmul(misc[:, 0:SB], wo[:, j, :], on[:, j * SB:(j + 1) * SB],
                                start=(j == 0), stop=(j == H // 2 - 1))
            last.then_inc(ys, 1)

    def tensor_block(e, g, nb, p, first, last):
        T, n, q = TensorSide(e), g + 1, 1 - p
        for k in range(16):
            if k == 0:
                if first:
                    e.wait_ge(xs, at(g, 1, 0))
                e.wait_ge(mn, at(g, 1, 1))
                T.project_q(n, 0)
            if k == 1:
                e.wait_ge(qs, at(n, 2, 1))
                T.project_q(n, 1)
            T.scores(g, p, k)
            if k > 0:
                T.values(g, k - 1)
            elif not first:
                T.values(g - 1, 15)
            if k == 3 and not first:
                e.wait_ge(qs, at(n, 2, 2))
                T.sums(g - 1, 1)
            if k == 7 and not first:
                T.project_out(g - 1)
            if k in starts:
                for j in range(*starts[k]):
                    T.row_scores(n, nb, q, j)
            if k == 11:
                e.wait_ge(*((qs, at(n, 2, 2)) if first else (xs, at(g - 1, 1, 1))))
                T.sums(g, 0)
            if k == 13:
                e.wait_ge(lg, at(g, 2, 1))
                T.turn_max(n)
        if last:
            T.values(g, 15)
            e.wait_ge(mn, at(n, 1, 1))
            T.sums(g, 1)
            e.wait_ge(lg, at(g, 2, 2))
            T.project_out(g)

    class ScalarSide:
        def __init__(self, e):
            self.e = e

        def split_q(self, n, p, u):
            e = self.e
            e.wait_ge(qp, at(n, 2, u + 1))
            e.wait_ge(qlo, at(n, 2, u))
            e.wait_ge(q2s, at(n, 2, u))
            for slot in range(4):
                sl = slice(slot * SB, (slot + 1) * SB)
                ins = e.activation(qf[:, sl], misc[:, sl], ACT.Identity, bias=bq[:, 4 * u + slot:4 * u + slot + 1])
            ins.then_inc(qs, 1)
            e.wait_ge(qs, at(n, 2, u + 1))
            for dst, done in ((q1[p], qhi), (q2[p], q2s)):
                for par in range(2):
                    rows, c = slice(par * HALF, (par + 1) * HALF), (2 * par + u) * SET
                    ins = e.activation(dst[rows, c:c + SET], qf[rows, :], ACT.Copy)
                ins.then_inc(done, 1)

        def exps(self, g, k):
            e = self.e
            e.wait_ge(st, at(g, 16, k + 1))
            e.wait_ge(pv, at(g, 16, k + 1 - NP))
            c = k % 8
            if c < 6:
                e.wait_ge(pa, at(g, 10, 5 * (k // 8 - 1) + max(c, 1)))
            else:
                e.wait_ge(da, at(g, 4, 2 * (k // 8 - 1) + 1))
            e.activation(pr[k % NP][:, :], bank[k % 2][:, :], ACT.Exp, scale=DK ** -0.5).then_inc(ex, 1)

        def out_values(self, g, u):
            e = self.e
            e.wait_ge(pv, at(g, 16, 8 * u + 8))
            e.wait_ge(od, at(g, 2, u))
            e.activation(osb[:, :], obank[:, :], ACT.Copy).then_inc(oe, 1)

        def invert(self, g, u):
            e = self.e
            e.wait_ge(ls, at(g, 2, u + 1))
            e.wait_ge(od, at(g, 2, u))
            e.activation(inv[:, :], misc[:, :], ACT.Ln).then_inc(lg, 1)
            e.wait_ge(lg, at(g, 2, u + 1))
            e.activation(inv[:, :], inv[:, :], ACT.Exp, scale=-1.0).then_inc(rc, 1)

        def negate_max(self, n):
            e = self.e
            e.wait_ge(mt, at(n, 1, 1))
            e.wait_ge(md, at(n, 32, 0))
            e.activation(mneg[:, :], misc[0:H, 0:SB], ACT.Copy, scale=-1.0).then_inc(mn, 1)

    def scalar_block(e, g, nb, p, first, last):
        A, n, q = ScalarSide(e), g + 1, 1 - p
        for k in range(16):
            A.exps(g, k)
            if k in (0, 1):
                if k == 0 and not first:
                    A.out_values(g - 1, 1)
                A.split_q(n, q, k)
            if k == 3 and not first:
                A.invert(g - 1, 1)
            if k == 8:
                A.out_values(g, 0)
            if k == 11:
                A.invert(g, 0)
            if k == 13:
                A.negate_max(n)
        if last:
            A.out_values(g, 1)
            A.invert(g, 1)

    class VectorSide:
        def __init__(self, e):
            self.e = e

        def low_q(self, n, p, u):
            e = self.e
            e.wait_ge(qhi, at(n, 2, u + 1))
            for par in range(2):
                rows, other = slice(par * HALF, (par + 1) * HALF), slice((1 - par) * HALF, (2 - par) * HALF)
                c = (2 * par + u) * SET
                ins = e.tensor_tensor(q1[p][other, c:c + SET], qf[rows, :], q1[p][rows, c:c + SET], ALU.subtract)
            ins.then_inc(qlo, 1)

        def row_max(self, n, j):
            e, h, half = self.e, j // 2, j % 2
            e.wait_ge(ms, at(n, 32, j + 1))
            if j == 0:
                e.wait_ge(mc, at(n, 1, 0))
            m = (h % 2) * 8 + h // 2
            e.tensor_reduce(mx[:, half, m:m + 1], row[:, half * TILE:(half + 1) * TILE], AX.X, ALU.max).then_inc(mr, 1)

        def join_max(self, n):
            e = self.e
            e.wait_ge(mr, at(n, 32, 32))
            e.wait_ge(mt, at(n, 1, 0))
            e.tensor_tensor(mrow[:, :], mx[:, 0, :], mx[:, 1, :], ALU.max).then_inc(mc, 1)

        def total_sums(self, g, u, stage):
            e = self.e
            if stage == 0:
                e.wait_ge(ex, at(g, 16, 8 * u + 8))
                e.wait_ge(ls, at(g, 2, u))
                e.tensor_tensor(total[:, :], pr[6][:, :], pr[7][:, :], ALU.add).then_inc(da, 1)
            else:
                e.wait_ge(pa, at(g, 10, 5 * u + 5))
                e.wait_ge(da, at(g, 4, 2 * u + 1))
                e.tensor_tensor(total[:, :], total[:, :], part[:, :], ALU.add).then_inc(da, 1)

        def normalise(self, g, u):
            e = self.e
            e.wait_ge(rc, at(g, 2, u + 1))
            e.wait_ge(oe, at(g, 2, u + 1))
            if u == 0:
                e.wait_ge(ys, at(g, 1, 0))
            e.tensor_tensor(on[:, u * SET:(u + 1) * SET], osb[:, :], inv[:, :], ALU.mult).then_inc(od, 1)

        def update_x(self, g, b):
            e = self.e
            e.wait_ge(ys, at(g, 1, 1))
            e.tensor_scalar(y[:, :], misc[:, 0:SB], bo[:, 0:1], mods[:, 0, 2, bass.ds(b, 1)],
                            ALU.add, ALU.mult).then_inc(yb, 1)
            e.wait_ge(yb, at(g, 1, 1))
            xb = x[:, bass.ds(g * SB, SB)]
            e.tensor_tensor(xb, xb, y[:, :], ALU.add).then_inc(xs, 1)

    def vector_block(e, g, b, p, first, last):
        V, n, q = VectorSide(e), g + 1, 1 - p
        for k in range(16):
            if k == 1 and not first:
                V.total_sums(g - 1, 1, 0)
            if k == 2 and not first:
                V.total_sums(g - 1, 1, 1)
            if k in (1, 2):
                V.low_q(n, q, k - 1)
            if k == 4 and not first:
                V.normalise(g - 1, 1)
            if k == 8 and not first:
                V.update_x(g - 1, b)
            if k == 9:
                V.total_sums(g, 0, 0)
            if k == 10:
                V.total_sums(g, 0, 1)
            if k in starts:
                for j in range(*starts[k]):
                    V.row_max(n, j)
            if k == 11:
                V.join_max(n)
            if k == 12:
                V.normalise(g, 0)
        if last:
            V.total_sums(g, 1, 0)
            V.total_sums(g, 1, 1)
            V.normalise(g, 1)
            V.update_x(g, b)

    def pool_block(e, g, b, p, first, last):
        for u in range(2):
            for c in range(1, 6):
                e.wait_ge(ex, at(g, 16, 8 * u + c + 1))
                if c == 1:
                    e.wait_ge(da, at(g, 4, 2 * u))
                e.wait_ge(pa, at(g, 10, 5 * u + c - 1))
                e.tensor_tensor(part[:, :], pr[0][:, :] if c == 1 else part[:, :], pr[c][:, :],
                                ALU.add).then_inc(pa, 1)

    def sync_block(e, g, nb, p, first, last):
        send_max(e, g + 1, 1 - p)

    def send_max(e, n, p):
        e.wait_ge(mn, at(n, 1, 1))
        for par in range(2):
            r = HALF * (1 - par)
            dst = q2[p][r:r + 1, par * 2 * SET:(par + 1) * 2 * SET]
            e.dma_start(dst.bitcast(F32), mneg[par * 8:par * 8 + 8, :].bitcast(F32)).then_inc(md, 16)

    def blocks(e, b, block, batch_of_next):
        g0 = b * BPB
        block(e, g0, b, 0, True, False)
        with e.Fori(0, (BPB - 2) // 2) as i:
            block(e, g0 + 1 + 2 * i, b, 1, False, False)
            block(e, g0 + 2 + 2 * i, b, 0, False, False)
        block(e, g0 + BPB - 1, b + 1 if batch_of_next else b, 1, False, True)

    def sync(e):
        e.wait_ge(zs, 1)
        send_max(e, 0, 0)
        with e.Fori(0, B) as b:
            blocks(e, b, sync_block, False)
        e.wait_ge(md, at(NB, 32, 32))

    def gpsimd(e):
        for r in range(2):
            e.memset(q2[r][:, :].bitcast(F32), 0.0)
            e.memset(klo[r][:, :].bitcast(F32), 0.0)
        last = e.memset(part[:, :], 0.0)
        last.then_inc(zs, 1)
        e.wait_ge(zs, 1)
        for r in range(2):
            o = HALF * (1 - r)
            last = e.memset(klo[r][o:o + 1, :].bitcast(F32), 1.0)
        last.then_inc(zs, 1)
        with e.Fori(0, B) as b:
            blocks(e, b, pool_block, False)

    def scalar(e):
        A = ScalarSide(e)
        Norm.tables(e)
        for q_ in (ex, qs, qhi, q2s, mn, lg, rc, oe):
            e.sem_inc(q_, BIAS)
        e.wait_ge(zs, 1)
        for u in range(2):
            A.split_q(0, 0, u)
        A.negate_max(0)
        with e.Fori(0, B) as b:
            e.wait_ge(kc, at(b, 4, 4))
            blocks(e, b, scalar_block, False)

    def vector(e):
        V = VectorSide(e)
        for q_ in (qlo, mr, mc, da, od, yb, xs, kc, pa, md):
            e.sem_inc(q_, BIAS)
        for u in range(2):
            V.low_q(0, 0, u)
        for j in range(2 * H):
            V.row_max(0, j)
        V.join_max(0)
        e.wait_ge(zs, 2)
        with e.Fori(0, B) as b:
            e.wait_ge(pv, at(b, 128, 0))
            e.tensor_copy(khi[:, :], khi_all[:, bass.ds(b * S, S)]).then_inc(kc, 1)
            for r in range(2):
                rows = slice(r * HALF, (r + 1) * HALF)
                e.tensor_copy(klo[r][rows, :], klo_all[rows, bass.ds(b * S, S)]).then_inc(kc, 1)
            e.tensor_copy(v[:, :], v_all[:, bass.ds(b * KC * DK, KC * DK)]).then_inc(kc, 1)
            blocks(e, b, vector_block, False)

    def tensor(e):
        T = TensorSide(e)
        for q_ in (st, pv, qp, ms, mt, ls, ys):
            e.sem_inc(q_, BIAS)
        T.project_q(0, 0)
        e.wait_ge(qs, at(0, 2, 1))
        T.project_q(0, 1)
        for j in range(2 * H):
            T.row_scores(0, 0, 0, j)
        e.wait_ge(qs, at(0, 2, 2))
        T.turn_max(0)
        with e.Fori(0, B) as b:
            e.wait_ge(kc, at(b, 4, 4))
            blocks(e, b, tensor_block, True)

    phase(prog, dict(sync=sync, gpsimd=gpsimd, scalar=scalar, vector=vector, tensor=tensor))


def twist_net(prog):
    nc, a, x, mods = prog.nc, prog.a, prog.x, prog.mods
    CYCLES, GROUPS, BIAS = 3, 2, 16
    D1, D2, D3 = P, P // 2, P // 4
    with ExitStack() as ctx:
        sb = lambda name, shape, dt=F32: prog.sb(ctx, f"tw_{name}", shape, dt)
        sem = lambda n: prog.sem(f"tw_{n}")
        o = sb("o", [P, N])
        w1, w2, w3 = sb("w1", [P, D1]), sb("w2", [P, D2]), sb("w3", [P, 2 * D3])
        w4 = sb("w4", [P, 4, P])
        w4c, b1, b2, b3, b4 = (sb(n, [P, 1]) for n in ("w4c", "b1", "b2", "b3", "b4"))
        g1, g2, g3c, g3 = sb("g1", [P, D2]), sb("g2", [D2, D3]), sb("g3c", [D3, 1]), sb("g3", [D3, P])
        c1, c2, c3 = sb("c1", [D2, 1]), sb("c2", [D3, 1]), sb("c3", [P, 1])
        rng, base, slope = sb("rng", [P, 1]), sb("base", [P, B]), sb("slope", [P, 1])
        tok = sb("tok", [P, 2, B])
        m, ga1, ga2, gt = sb("m", [P, B]), sb("ga1", [D2, B]), sb("ga2", [D3, B]), sb("gt", [P, B])
        turn = sb("turn", [P, P])
        a1 = [sb(f"a1_{g}", [P, 4 * TILE]) for g in range(GROUPS)]
        a2 = [sb(f"a2_{g}", [P, 2 * TILE]) for g in range(GROUPS)]
        a3 = [sb(f"a3_{g}", [P, TILE]) for g in range(GROUPS)]
        tt = [sb(f"tt_{g}", [P, 4 * TILE]) for g in range(GROUPS)]
        norm = Norm(prog, ctx, "ln1", 0, 1)
        loaded, late, consts, s_h, s_w, gp, gv, gs = (sem(n) for n in (
            "loaded", "late", "consts", "h", "weights", "g_product", "g_vector", "g_gelu"))

        def sync(e):
            for dst, name in ((w1, "cn_w1"), (w2, "cn_w2"), (g1, "gc_w1"), (g2, "gc_w2"), (g3c, "gc_w3")):
                e.dma_start(dst[:, :], a[f"L0_ffn_{name}"]).then_inc(loaded, 16)
            col = lambda name: a[f"L0_ffn_{name}"].unsqueeze(1)
            for dst, name in ((b1, "cn_b1"), (c1, "gc_b1"), (c2, "gc_b2")):
                e.dma_start(dst[:, :], col(name)).then_inc(loaded, 16)
            for r in range(2):
                e.dma_start(b2[r * D2:(r + 1) * D2, :], col("cn_b2")).then_inc(loaded, 16)
            for r in range(4):
                rows = slice(r * D3, (r + 1) * D3)
                e.dma_start(b3[rows, :], col("cn_b3")).then_inc(loaded, 16)
                e.dma_start(w4c[rows, :], a["L0_ffn_cn_w4"]).then_inc(loaded, 16)
            for dst, name in ((b4, "cn_b4"), (c3, "gc_b3"), (rng, "adaptive_range")):
                e.dma_start(dst[:, :], a[f"L0_ffn_{name}"].partition_broadcast(P)).then_inc(loaded, 16)
            e.wait_ge(consts, 1)
            for r in range(2):
                e.dma_start(w3[r * D2:(r + 1) * D2, r * D3:(r + 1) * D3], a["L0_ffn_cn_w3"]).then_inc(late, 16)
            e.wait_ge(late, 32)

        def gpsimd(e):
            e.memset(w3[:, :], 0.0).then_inc(consts, 1)
            e.memset(w4[:, :, :], 0.0).then_inc(consts, 1)
            e.memset(turn[:, :], 0.0).then_inc(consts, 1)
            e.wait_ge(consts, 3)
            for quad, (src, sign) in enumerate(((2, 1.0), (3, -1.0), (0, -1.0), (1, 1.0))):
                cols = turn[:, quad * D3:(quad + 1) * D3]
                e.affine_select(out=cols, in_=cols, compare_op=ALU.not_equal, fill=sign, base=-src * D3,
                                pattern=[[-1, D3]], channel_multiplier=1).then_inc(consts, 1)
            e.wait_ge(consts, 7)

        s1, s2, s3, s4, s5 = (sem(f"layer{i}") for i in (1, 2, 3, 4, 5))
        e1, e2, e3, e4 = (sem(f"act{i}") for i in (1, 2, 3, 4))
        dc, dt_, do = sem("coupling"), sem("step"), sem("out")
        dx = sem("x")
        at = lambda cyc, per, k: cyc * per + (BIAS + k)
        pair = lambda g, h: prog.pairs[2 * g + h]

        def tensor(e):
            with e.Fori(0, B) as b:
                norm.tensor(e, b)
            for q in (s1, s2, s3, s4, s5):
                e.sem_inc(q, BIAS)
            e.wait_ge(loaded, 16 * 21)
            e.wait_ge(s_w, 8)
            e.wait_ge(gv, 1)
            ps = prog.pairs[0]
            e.matmul(ps[0:D2, 0:B], g1[:, :], m[:, :], start=True, stop=True).then_inc(gp, 1)
            e.wait_ge(gs, 1)
            e.matmul(ps[0:D3, 8:8 + B], g2[:, :], ga1[:, :], start=True, stop=True).then_inc(gp, 1)
            e.wait_ge(gs, 2)
            e.matmul(ps[:, 16:16 + B], g3[:, :], ga2[:, :], start=True, stop=True).then_inc(gp, 1)
            e.wait_ge(gs, 3)
            e.wait_ge(late, 32)
            e.wait_ge(consts, 7)
            with e.Fori(0, CYCLES) as cyc:
                for g in range(GROUPS):
                    for h in range(2):
                        e.wait_ge(do, at(cyc, 4, 2 * g + h - 3))
                        for t in range(2):
                            c = (4 * g + 2 * h + t) * TILE
                            last = e.matmul(pair(g, h)[:, t * TILE:(t + 1) * TILE], w1[:, :], o[:, c:c + TILE],
                                            start=True, stop=True)
                        last.then_inc(s1, 1)
                for g in range(GROUPS):
                    e.wait_ge(e1, at(cyc, 4, 2 * g + 2))
                    for k in range(4):
                        last = e.matmul(pair(g, 0)[(k % 2) * D2:(k % 2 + 1) * D2, (k // 2) * TILE:(k // 2 + 1) * TILE],
                                        w2[:, :], a1[g][:, k * TILE:(k + 1) * TILE], start=True, stop=True)
                    last.then_inc(s2, 1)
                for g in range(GROUPS):
                    e.wait_ge(e2, at(cyc, 2, g + 1))
                    for k in range(2):
                        last = e.matmul(pair(g, 1)[k * D2:(k + 1) * D2, 0:TILE], w3[:, :],
                                        a2[g][:, k * TILE:(k + 1) * TILE], start=True, stop=True)
                    last.then_inc(s3, 1)
                for g in range(GROUPS):
                    e.wait_ge(e3, at(cyc, 2, g + 1))
                    for k in range(4):
                        last = e.matmul(pair(g, k // 2)[:, (k % 2) * TILE:(k % 2 + 1) * TILE], w4[:, k, :],
                                        a3[g][:, :], start=True, stop=True)
                        if k % 2:
                            last.then_inc(s4, 1)
                for g in range(GROUPS):
                    for h in range(2):
                        e.wait_ge(e4, at(cyc, 4, 2 * g + h + 1))
                        for t in range(2):
                            c = (4 * g + 2 * h + t) * TILE
                            last = e.matmul(pair(g, h)[:, t * TILE:(t + 1) * TILE], turn[:, :], o[:, c:c + TILE],
                                            start=True, stop=True)
                        last.then_inc(s5, 1)

        def scalar(e):
            norm.tables(e)
            with e.Fori(0, B) as b:
                norm.scalar(e, b)
                for c in range(2):
                    norm.affine(e, b, c, o[:, bass.ds(b * S + c * TILE, TILE)],
                                accum=tok[:, c, bass.ds(b, 1)]).then_inc(s_h, 1)
            for q in (e1, e2, e3, e4):
                e.sem_inc(q, BIAS)
            ps = prog.pairs[0]
            e.preload_act_table_set("gelu_and_others")
            e.wait_ge(loaded, 16 * 21)
            for n, (dst, src, bias) in enumerate(((ga1[:, :], ps[0:D2, 0:B], c1), (ga2[:, :], ps[0:D3, 8:8 + B], c2))):
                e.wait_ge(gp, n + 1)
                e.activation(dst, src, ACT.Gelu, bias=bias[:, 0:1]).then_inc(gs, 1)
            e.wait_ge(gp, 3)
            e.wait_ge(s_w, 8)
            e.activation(gt[:, :], ps[:, 16:16 + B], ACT.Tanh, scale=0.5, bias=c3[:, 0:1]).then_inc(gs, 1)
            with e.Fori(0, CYCLES) as cyc:
                for g in range(GROUPS):
                    for h in range(2):
                        e.wait_ge(s1, at(cyc, 4, 2 * g + h + 1))
                        e.activation(a1[g][:, 2 * h * TILE:2 * (h + 1) * TILE], pair(g, h)[:, :], ACT.Gelu,
                                     bias=b1[:, 0:1]).then_inc(e1, 1)
                for g in range(GROUPS):
                    e.wait_ge(s2, at(cyc, 2, g + 1))
                    e.activation(a2[g][:, :], pair(g, 0)[:, :], ACT.Gelu, bias=b2[:, 0:1]).then_inc(e2, 1)
                for g in range(GROUPS):
                    e.wait_ge(s3, at(cyc, 2, g + 1))
                    e.activation(a3[g][:, :], pair(g, 1)[:, 0:TILE], ACT.Gelu, bias=b3[:, 0:1]).then_inc(e3, 1)
                for g in range(GROUPS):
                    for h in range(2):
                        e.wait_ge(s4, at(cyc, 4, 2 * g + h + 1))
                        e.wait_ge(dt_, at(cyc, 4, 2 * g + h - 3))
                        e.activation(tt[g][:, 2 * h * TILE:2 * (h + 1) * TILE], pair(g, h)[:, :], ACT.Tanh,
                                     scale=0.5, bias=b4[:, 0:1]).then_inc(e4, 1)

        def vector(e):
            e.wait_ge(loaded, 16 * 21)
            v = Chain(s_w)
            e.wait_ge(consts, 2)
            for k in range(4):
                rows = slice(k * D3, (k + 1) * D3)
                v.inc(e.tensor_copy(w4[rows, k, :], w4c[rows, 0:1].to_broadcast([D3, P])))
            v.inc(e.tensor_copy(g3[:, :], g3c[:, 0:1].to_broadcast([D3, P])))
            v.inc(e.tensor_scalar(b4[:, :], b4[:, :], 0.5, None, ALU.mult))
            v.inc(e.tensor_scalar(c3[:, :], c3[:, :], 0.5, None, ALU.mult))
            e.wait_ge(s_w, v.inc(e.tensor_scalar(slope[:, :], rng[:, :], 0.3, None, ALU.mult)))
            with e.Fori(0, B) as b:
                norm.vector(e, b)
            for q in (dc, dt_, do, dx):
                e.sem_inc(q, BIAS)
            e.wait_ge(s_h, 2 * B)
            e.wait_ge(s_w, v.inc(e.tensor_tensor(m[:, :], tok[:, 0, :], tok[:, 1, :], ALU.add)))
            e.tensor_scalar(m[:, :], m[:, :], 1.0 / S, None, ALU.mult).then_inc(gv, 1)
            e.wait_ge(gs, 3)
            e.wait_ge(s_w, v.inc(e.tensor_scalar(base[:, :], gt[:, :], rng[:, 0:1], 0.7, ALU.mult, ALU.mult)))
            e.wait_ge(s_w, v.inc(e.tensor_scalar(base[:, :], base[:, :], 0.1, None, ALU.add)))
            with e.Fori(0, CYCLES) as cyc:
                for g in range(GROUPS):
                    for h in range(2):
                        k = 2 * g + h
                        t_ = tt[g][:, 2 * h * TILE:2 * (h + 1) * TILE]
                        ob = o[:, k * S:(k + 1) * S]
                        e.wait_ge(e4, at(cyc, 4, k + 1))
                        e.tensor_scalar(t_, t_, slope[:, 0:1], base[:, k:k + 1], ALU.mult, ALU.add).then_inc(dc, 1)
                        e.wait_ge(dc, at(cyc, 4, k + 1))
                        e.wait_ge(s5, at(cyc, 4, k + 1))
                        e.tensor_tensor(t_, pair(g, h)[:, :], t_, ALU.mult).then_inc(dt_, 1)
                        e.wait_ge(dt_, at(cyc, 4, k + 1))
                        e.tensor_tensor(ob, ob, t_, ALU.add).then_inc(do, 1)
                        e.wait_ge(do, at(cyc, 4, k + 1))
            for b in range(B):
                xb = x[:, b * S:(b + 1) * S]
                e.scalar_tensor_tensor(out=xb, in0=o[:, b * S:(b + 1) * S], scalar=mods[:, 0, 5, b:b + 1],
                                       in1=xb, op0=ALU.mult, op1=ALU.add).then_inc(dx, 1)

        phase(prog, dict(sync=sync, gpsimd=gpsimd, scalar=scalar, vector=vector, tensor=tensor))


def attention1(prog):
    nc, a, x, mods = prog.nc, prog.a, prog.x, prog.mods
    WT = TILE // W
    BT = WT // 2
    BB = 2 * BT
    BIAS = 32
    with ExitStack() as ctx:
        sb = lambda name, shape, dt=F32: prog.sb(ctx, f"w_{name}", shape, dt)
        sem = lambda n: prog.sem(f"w_{n}")
        wi, wo = sb("wi", [P, 3 * P]), sb("wo", [P, P])
        bi, bo = sb("bi", [P, 3]), sb("bo", [P, 1])
        gate = sb("gate", [P, B])
        hmask = sb("hmask", [P, HEADS])
        vmask = sb("vmask", [P, P])
        hr = sb("hr", [P, 2, TILE])
        q = [sb(f"q{c}", [P, TILE]) for c in range(2)]
        kb = [sb(f"k{c}", [P, TILE]) for c in range(2)]
        kx = [sb(f"kx{c}", [P, WT, HEADS, W]) for c in range(2)]
        vx = [sb(f"vx{c}", [P, WT, P]) for c in range(2)]
        d = [sb(f"d{i}", [P, HEADS * W]) for i in range(2)]
        pn = [sb(f"pn{i}", [P, HEADS * W]) for i in range(2)]
        pt = [sb(f"pt{i}", [P, HEADS * W]) for i in range(2)]
        mx, sm, rs = sb("mx", [P, 2, HEADS]), sb("sm", [P, 2, HEADS]), sb("rs", [P, 2, HEADS])
        ob = [sb(f"ob{c}", [P, TILE]) for c in range(2)]
        yb = [sb(f"yb{c}", [P, TILE]) for c in range(2)]
        norm = Norm(prog, ctx, "ln2", 1, 0)
        loaded, consts = sem("loaded"), sem("consts")

        def sync(e):
            e.dma_start(wi[:, :], a["L1_attn_in_proj_w"]).then_inc(loaded, 16)
            e.dma_start(wo[:, :], a["L1_attn_out_w"]).then_inc(loaded, 16)
            e.dma_start(bi[:, :], a["L1_attn_in_proj_b"]).then_inc(loaded, 16)
            e.dma_start(bo[:, :], a["L1_attn_out_b"].unsqueeze(1)).then_inc(loaded, 16)
            e.wait_ge(loaded, 64)

        hs = sem("h")
        qp, kp = sem("q"), sem("k")
        qb, kbs = sem("q_biased"), sem("k_biased")
        kxs, vp, vxs = sem("k_spread"), sem("v"), sem("v_spread")
        sp, m_, dd, ee, ss, rr, nn, tp, tc, op = (sem(n) for n in (
            "scores", "max", "shifted", "exps", "sum", "inverse", "probs", "probs_T", "probs_T_out", "pv"))
        oc, yp, yy, xx = sem("pv_out"), sem("y"), sem("y_biased"), sem("x")
        at = lambda b, per, k: b * per + (BIAS + k)
        qk_ps = [prog.pairs[0][:, i * TILE:(i + 1) * TILE] for i in range(2)]
        s_ps = [prog.pairs[1][:, i * TILE:(i + 1) * TILE] for i in range(2)]
        t_ps = [prog.pairs[2][:, i * TILE:(i + 1) * TILE] for i in range(2)]
        v_ps, o_ps = prog.banks

        def gpsimd(e):
            e.memset(hmask[:, :], 1.0).then_inc(consts, 1)
            e.memset(vmask[:, :], 1.0).then_inc(consts, 1)
            e.wait_ge(consts, 2)
            e.affine_select(out=hmask[:, :], in_=hmask[:, :], compare_op=ALU.is_ge, fill=0.0, base=0,
                            pattern=[[-HD, HEADS]], channel_multiplier=1).then_inc(consts, 1)
            e.wait_ge(consts, 3)
            e.affine_select(out=hmask[:, :], in_=hmask[:, :], compare_op=ALU.is_ge, fill=0.0, base=HD - 1,
                            pattern=[[HD, HEADS]], channel_multiplier=-1).then_inc(consts, 1)
            e.wait_ge(consts, 4)
            for r in range(2):
                v = vmask[r * W:(r + 1) * W, :].rearrange("p (g a c) -> p g a c", a=2, c=HD)[:, :, 1 - r, :]
                e.memset(v, 0.0).then_inc(consts, 1)
            e.wait_ge(consts, 6)
            e.sem_inc(nn, BIAS)
            with e.Fori(0, B) as b:
                for j in range(BB):
                    e.wait_ge(rr, at(b, BB, j + 1))
                    e.wait_ge(tp, at(b, BB, j - 1))
                    i = j % 2
                    e.tensor_tensor(pn[i][:, :].rearrange("p (h k) -> p h k", k=W),
                                    d[i][:, :].rearrange("p (h k) -> p h k", k=W),
                                    rs[:, i, :].unsqueeze(2).to_broadcast([P, HEADS, W]), ALU.mult).then_inc(nn, 1)

        def tensor(e):
            def tile_in(b, c):
                e.wait_ge(hs, at(b, 4, 4 if c else 3))
                e.wait_ge(kxs, at(b, 2, c - 1))
                e.matmul(qk_ps[0], wi[:, 0:P], hr[:, c, :], start=True, stop=True).then_inc(qp, 1)
                e.matmul(qk_ps[1], wi[:, P:2 * P], hr[:, c, :], start=True, stop=True).then_inc(kp, 1)

            def values(b, c, half):
                e.wait_ge(vxs, at(b, 4, 2 * c + half))
                for w in range(4):
                    win = hr[:, c, (4 * half + w) * W:(4 * half + w + 1) * W]
                    for r in range(2):
                        last = e.matmul(v_ps[r * W:(r + 1) * W, w * P:(w + 1) * P], win, wi[:, 2 * P:3 * P],
                                        start=True, stop=True)
                last.then_inc(vp, 1)

            def scores(b, j):
                c, i = j // BT, j % 2
                if j % BT == 0:
                    e.wait_ge(qb, at(b, 2, c + 1))
                    e.wait_ge(kxs, at(b, 2, c + 1))
                e.wait_ge(dd, at(b, BB, j - 1))
                for w in range(2):
                    n = 2 * (j % BT) + w
                    last = e.matmul(s_ps[i][w * W:(w + 1) * W, :], q[c][:, n * W:(n + 1) * W],
                                    kx[c][:, n, :, :].rearrange("p h k -> p (h k)"), start=True, stop=True)
                last.then_inc(sp, 1)

            def turn(b, j):
                i = j % 2
                e.wait_ge(nn, at(b, BB, j + 1))
                e.wait_ge(tc, at(b, BB, j - 1))
                for r in range(4):
                    last = e.matmul(t_ps[i][:, r * P:(r + 1) * P], pn[i][:, r * P:(r + 1) * P], prog.ident[:, :],
                                    is_transpose=True)
                last.then_inc(tp, 1)

            def products(b, j):
                c, i = j // BT, j % 2
                e.wait_ge(tc, at(b, BB, j + 1))
                e.wait_ge(vxs, at(b, 4, 2 * c + 1 + (j % BT) // 2))
                if j % BT == 0:
                    e.wait_ge(oc, at(b, 2, c))
                for w in range(2):
                    n = 2 * (j % BT) + w
                    for r in range(4):
                        last = e.matmul(o_ps[r * 2 * HD:(r + 1) * 2 * HD, n * W:(n + 1) * W],
                                        vx[c][:, n, r * 2 * HD:(r + 1) * 2 * HD],
                                        pt[i][:, r * P + w * W:r * P + (w + 1) * W], start=True, stop=True)
                last.then_inc(op, 1)

            def tile_out(b, c):
                e.wait_ge(oc, at(b, 2, c + 1))
                e.wait_ge(yy, at(b, 2, c))
                e.matmul(y_ps, wo[:, :], ob[c][:, :], start=True, stop=True).then_inc(yp, 1)

            y_ps = qk_ps[0]
            for s_ in (qp, kp, vp, sp, tp, op, yp):
                e.sem_inc(s_, BIAS)
            with e.Fori(0, B) as b:
                e.wait_ge(yy, at(b, 2, 0))
                norm.tensor(e, b)
                e.wait_ge(loaded, 64)
                tile_in(b, 0)
                values(b, 0, 0)
                values(b, 0, 1)
                tile_in(b, 1)
                for j in range(BB + 2):
                    if j < BB:
                        scores(b, j)
                    if j in (2, 3):
                        values(b, 1, j - 2)
                    if 1 <= j <= BB:
                        turn(b, j - 1)
                    if j >= 2:
                        products(b, j - 2)
                    if j == BT + 3:
                        tile_out(b, 0)
                tile_out(b, 1)

        def scalar(e):
            for s_ in (hs, qb, kbs, ee, tc, oc, yy):
                e.sem_inc(s_, BIAS)
            e.wait_ge(loaded, 64)
            norm.tables(e)
            with e.Fori(0, B) as b:
                norm.scalar(e, b)
                e.wait_ge(vp, at(b, 4, 0))
                norm.affine(e, b, 0, hr[:, 0, 0:TILE - SHIFT], cols=(SHIFT, TILE)).then_inc(hs, 1)
                norm.affine(e, b, 0, hr[:, 1, TILE - SHIFT:TILE], cols=(0, SHIFT)).then_inc(hs, 1)
                norm.affine(e, b, 1, hr[:, 0, TILE - SHIFT:TILE], cols=(0, SHIFT)).then_inc(hs, 1)
                norm.affine(e, b, 1, hr[:, 1, 0:TILE - SHIFT], cols=(SHIFT, TILE)).then_inc(hs, 1)

                def tile_in(c):
                    e.wait_ge(qp, at(b, 2, c + 1))
                    e.wait_ge(sp, at(b, BB, (c - 1) * BT))
                    e.activation(q[c][:, :], qk_ps[0], ACT.Identity, bias=bi[:, 0:1]).then_inc(qb, 1)
                    e.wait_ge(kp, at(b, 2, c + 1))
                    e.wait_ge(kxs, at(b, 2, c - 1))
                    e.activation(kb[c][:, :], qk_ps[1], ACT.Identity, bias=bi[:, 1:2]).then_inc(kbs, 1)
                tile_in(0)
                tile_in(1)
                for j in range(BB + 2):
                    i = j % 2
                    if j < BB:
                        e.wait_ge(dd, at(b, BB, j + 1))
                        e.activation(d[i][:, :], d[i][:, :], ACT.Exp, scale=HD ** -0.5).then_inc(ee, 1)
                    if 1 <= j <= BB:
                        n = j - 1
                        e.wait_ge(tp, at(b, BB, n + 1))
                        e.wait_ge(op, at(b, BB, n - 1))
                        e.activation(pt[n % 2][:, :], t_ps[n % 2], ACT.Copy).then_inc(tc, 1)
                    if j in (BT + 2, BB + 1):
                        c = 0 if j == BT + 2 else 1
                        e.wait_ge(op, at(b, BB, (c + 1) * BT))
                        e.wait_ge(yp, at(b, 2, c - 1))
                        e.activation(ob[c][:, :], o_ps, ACT.Identity, bias=bi[:, 2:3]).then_inc(oc, 1)
                    if j == BT + 3:
                        tile_out(e, b, 0)
                tile_out(e, b, 1)

        def tile_out(e, b, c):
            e.wait_ge(yp, at(b, 2, c + 1))
            e.wait_ge(xx, at(b, 2, c - 1))
            e.activation(yb[c][:, :], qk_ps[0], ACT.Identity, bias=bo[:, 0:1]).then_inc(yy, 1)

        def vector(e):
            e.wait_ge(consts, 6)
            gd = sem("gate_doubled")
            e.tensor_scalar(gate[:, :], mods[:, 1, 2, :], 2.0, None, ALU.mult).then_inc(gd, 1)
            e.wait_ge(gd, 1)
            for s_ in (kxs, vxs, m_, dd, ss, rr, xx):
                e.sem_inc(s_, BIAS)
            with e.Fori(0, B) as b:
                norm.vector(e, b)

                def spread_k(c):
                    e.wait_ge(kbs, at(b, 2, c + 1))
                    e.wait_ge(sp, at(b, BB, (c - 1) * BT))
                    for h in range(HEADS):
                        last = e.tensor_scalar(kx[c][:, :, h, :], kb[c][:, :].rearrange("p (w k) -> p w k", k=W),
                                               hmask[:, h:h + 1], None, ALU.mult)
                    last.then_inc(kxs, 1)

                def spread_v(c, half):
                    e.wait_ge(vp, at(b, 4, 2 * c + half + 1))
                    e.wait_ge(op, at(b, BB, (c - 1) * BT))
                    e.tensor_tensor(vx[c][:, 4 * half:4 * half + 4, :], v_ps.rearrange("p (w f) -> p w f", f=P),
                                    vmask[:, :].unsqueeze(1).to_broadcast([P, 4, P]), ALU.mult).then_inc(vxs, 1)

                def shift(j):
                    i = j % 2
                    s3 = s_ps[i].rearrange("p (h k) -> p h k", k=W)
                    e.wait_ge(sp, at(b, BB, j + 1))
                    e.wait_ge(dd, at(b, BB, j - 1))
                    e.tensor_reduce(mx[:, i, :], s3, AX.X, ALU.max).then_inc(m_, 1)
                    e.wait_ge(m_, at(b, BB, j + 1))
                    e.wait_ge(nn, at(b, BB, j - 1))
                    e.tensor_tensor(d[i][:, :].rearrange("p (h k) -> p h k", k=W), s3,
                                    mx[:, i, :].unsqueeze(2).to_broadcast([P, HEADS, W]),
                                    ALU.subtract).then_inc(dd, 1)

                def invert(j):
                    i = j % 2
                    e.wait_ge(ee, at(b, BB, j + 1))
                    e.tensor_reduce(sm[:, i, :], d[i][:, :].rearrange("p (h k) -> p h k", k=W), AX.X,
                                    ALU.add).then_inc(ss, 1)
                    e.wait_ge(ss, at(b, BB, j + 1))
                    e.wait_ge(nn, at(b, BB, j - 1))
                    e.reciprocal(rs[:, i, :], sm[:, i, :]).then_inc(rr, 1)

                def update(c):
                    e.wait_ge(yy, at(b, 2, c + 1))
                    parts = ((SHIFT, 0, TILE),) if c == 0 else ((TILE + SHIFT, 0, TILE - SHIFT), (0, TILE - SHIFT, SHIFT))
                    for to, frm, n in parts:
                        xb = x[:, bass.ds(b * S + to, n)]
                        last = e.scalar_tensor_tensor(out=xb, in0=yb[c][:, frm:frm + n], scalar=gate[:, bass.ds(b, 1)],
                                                      in1=xb, op0=ALU.mult, op1=ALU.add)
                    last.then_inc(xx, 1)
                spread_k(0)
                spread_v(0, 0)
                spread_v(0, 1)
                spread_k(1)
                for j in range(BB + 1):
                    if j < BB:
                        shift(j)
                    if j in (2, 3):
                        spread_v(1, j - 2)
                    if j >= 1:
                        invert(j - 1)
                    if j == BB - 1:
                        update(0)
                update(1)

        phase(prog, dict(sync=sync, gpsimd=gpsimd, scalar=scalar, vector=vector, tensor=tensor))


def experts(prog):
    nc, a, x, mods = prog.nc, prog.a, prog.x, prog.mods
    BT = TILE // P
    GE = NB * E
    with ExitStack() as ctx:
        sb = lambda name, shape, dt=F32: prog.sb(ctx, f"x_{name}", shape, dt)
        sem = lambda n: prog.sem(f"x_{n}")
        h = sb("h", [P, N])
        hfix = sb("hfix", [P, 2, TILE])
        wg, w1 = sb("wg", [P, E]), sb("w1", [P, E, HID])
        w2, b1 = sb("w2", [P, E * HC, P]), sb("b1", [P, E * HC])
        b2 = sb("b2", [E, P])
        norm = Norm(prog, ctx, "ln3", 1, 1)
        lg = sb("lg", [P, GE])
        gates = sb("gates", [P, GE])
        gt = sb("gt", [E, N])
        loaded, hs, hf, lp = sem("loaded"), sem("h"), sem("hfix"), sem("logits")
        lg_ps = prog.banks[0]

        def sync(e):
            e.dma_start(wg[:, :], a["L1_ffn_Wg"]).then_inc(loaded, 16)
            e.dma_start(w1[:, :, :], a["L1_ffn_W1"].rearrange("e p h -> p e h")).then_inc(loaded, 16)
            e.dma_start(w2[:, :, :], a["L1_ffn_W2"].rearrange("e (c p) f -> p (e c) f", p=P)).then_inc(loaded, 16)
            e.dma_start(b1[:, :], a["L1_ffn_b1"]).then_inc(loaded, 16)
            e.dma_start(b2[:, :], a["L1_ffn_b2"]).then_inc(loaded, 16)
            e.wait_ge(loaded, 80)

        lo = sem("logits_out")

        def tensor(e):
            with e.Fori(0, B) as b:
                norm.tensor(e, b)
                e.wait_ge(loaded, 80)
                for c in range(BPB):
                    if c % BT == 0:
                        e.wait_ge(hf, 2 * b + c // BT + 1)
                    last = e.matmul(lg_ps[:, c * E:(c + 1) * E], hfix[:, c // BT, (c % BT) * P:(c % BT + 1) * P],
                                    wg[:, :], start=True, stop=True)
                last.then_inc(lp, 1)
                e.wait_ge(lo, b + 1)

        def scalar(e):
            norm.tables(e)
            with e.Fori(0, B) as b:
                norm.scalar(e, b)
                for c in range(2):
                    norm.affine(e, b, c, h[:, bass.ds(b * S + c * TILE, TILE)]).then_inc(hs, 1)
                    norm.affine(e, b, c, hfix[:, c, :]).then_inc(hf, 1)

        def vector(e):
            with e.Fori(0, B) as b:
                norm.vector(e, b)
                e.wait_ge(lp, b + 1)
                e.tensor_copy(lg[:, bass.ds(b * BPB * E, BPB * E)], lg_ps[:, 0:BPB * E]).then_inc(lo, 1)

        phase(prog, dict(sync=sync, scalar=scalar, vector=vector, tensor=tensor))
        gate_tokens(prog, lg, gates, gt)
        run_experts(prog, h, w1, w2, b1, b2, gates, gt)


def gate_tokens(prog, lg, gates, gt):
    GE = NB * E
    with ExitStack() as ctx:
        sb = lambda name, shape, dt=F32: prog.sb(ctx, f"g_{name}", shape, dt)
        sem = lambda n: prog.sem(f"g_{n}")
        ramp, before, m = sb("ramp", [P, E]), sb("before", [P, P]), sb("m", [P, GE])
        eq, m1, m2, lg2, ex = (sb(n, [P, GE]) for n in ("eq", "m1", "m2", "lg2", "ex"))
        tot = [sb(f"tot{i}", [P, NB + 1, E]) for i in range(2)]
        v1, v2, km, z = (sb(n, [P, NB]) for n in ("v1", "v2", "km", "z"))
        made, s_v, s_p, s_a = sem("made"), sem("vector"), sem("product"), sem("exp")
        cnt_ps, tot_ps = prog.pairs[0][:, 0:GE], prog.pairs[0][:, TILE:TILE + GE]
        by = lambda ap: ap.rearrange("p (n e) -> p n e", e=E)
        spread = lambda ap: ap.unsqueeze(2).to_broadcast([P, NB, E])
        marks = {}

        def gpsimd(e):
            for k in range(E):
                e.memset(ramp[:, k:k + 1], float(E - k))
            e.memset(before[:, :], 1.0).then_inc(made, 1)
            e.wait_ge(made, 1)
            e.affine_select(out=before[:, :], in_=before[:, :], compare_op=ALU.is_ge, fill=0.0, base=-1,
                            pattern=[[1, P]], channel_multiplier=-1).then_inc(made, 1)
            e.wait_ge(made, 2)

        def vector(e):
            v = Chain(s_v)
            step = lambda ins: e.wait_ge(s_v, v.inc(ins))
            e.wait_ge(made, 2)

            def pick(src, top, mask):
                step(e.tensor_reduce(top[:, :], by(src[:, :]), AX.X, ALU.max))
                step(e.tensor_tensor(by(eq[:, :]), by(src[:, :]), spread(top[:, :]), ALU.is_equal))
                step(e.tensor_tensor(by(eq[:, :]), by(eq[:, :]),
                                     ramp[:, :].unsqueeze(1).to_broadcast([P, NB, E]), ALU.mult))
                step(e.tensor_reduce(km[:, :], by(eq[:, :]), AX.X, ALU.max))
                step(e.tensor_tensor(by(mask[:, :]), by(eq[:, :]), spread(km[:, :]), ALU.is_equal))
            pick(lg, v1, m1)
            step(e.scalar_tensor_tensor(out=lg2[:, :], in0=m1[:, :], scalar=-BIG, in1=lg[:, :],
                                        op0=ALU.mult, op1=ALU.add))
            pick(lg2, v2, m2)
            step(e.tensor_tensor(m[:, :], m1[:, :], m2[:, :], ALU.add))
            marks["m"] = v.n
            step(e.tensor_tensor(by(ex[:, :]), by(lg[:, :]), spread(v1[:, :]), ALU.subtract))
            marks["ex"] = v.n
            step(e.memset(tot[0][:, 0:1, :], 0.0))
            step(e.memset(tot[1][:, 0:1, :], 0.0))
            e.wait_ge(s_p, 1)
            step(e.tensor_copy(tot[0][:, 1:NB + 1, :], by(tot_ps)))
            cur, reach = 0, 1
            while reach < NB:
                old, new = tot[cur], tot[1 - cur]
                step(e.tensor_copy(new[:, 1:1 + reach, :], old[:, 1:1 + reach, :]))
                step(e.tensor_tensor(new[:, 1 + reach:NB + 1, :], old[:, 1 + reach:NB + 1, :],
                                     old[:, 1:NB + 1 - reach, :], ALU.add))
                cur, reach = 1 - cur, 2 * reach
            step(e.tensor_tensor(by(eq[:, :]), by(cnt_ps), tot[cur][:, 0:NB, :], ALU.add))
            step(e.tensor_scalar(eq[:, :], eq[:, :], float(CAP), None, ALU.is_lt))
            e.wait_ge(s_a, 1)
            step(e.tensor_reduce(z[:, :], by(ex[:, :]), AX.X, ALU.add))
            step(e.reciprocal(z[:, :], z[:, :]))
            step(e.tensor_tensor(by(ex[:, :]), by(ex[:, :]), spread(z[:, :]), ALU.mult))
            step(e.tensor_tensor(ex[:, :], ex[:, :], m[:, :], ALU.mult))
            step(e.tensor_reduce(z[:, :], by(ex[:, :]), AX.X, ALU.add))
            step(e.reciprocal(z[:, :], z[:, :]))
            step(e.tensor_tensor(by(ex[:, :]), by(ex[:, :]), spread(z[:, :]), ALU.mult))
            step(e.tensor_tensor(gates[:, :], ex[:, :], eq[:, :], ALU.mult))
            marks["gates"] = v.n
            for i in range(NB // 4):
                e.wait_ge(s_p, 2 + i)
                e.tensor_copy(gt[:, i * TILE:(i + 1) * TILE], prog.pairs[1 + i // 2][0:E, (i % 2) * TILE:(i % 2 + 1) * TILE]
                              if i < 6 else prog.pairs[0][0:E, (i % 2) * TILE:(i % 2 + 1) * TILE]).then_inc(s_v, 1)
            e.wait_ge(s_v, v.n + NB // 4)

        def scalar(e):
            e.wait_ge(s_v, marks_ex)
            e.activation(ex[:, :], ex[:, :], ACT.Exp).then_inc(s_a, 1)

        def tensor(e):
            e.wait_ge(s_v, marks_m)
            e.matmul(cnt_ps, before[:, :], m[:, :], start=True, stop=True)
            e.matmul(tot_ps, prog.ones[:, :], m[:, :], start=True, stop=True).then_inc(s_p, 1)
            e.wait_ge(s_v, marks_gates)
            for i in range(NB // 4):
                ps = prog.pairs[1 + i // 2] if i < 6 else prog.pairs[0]
                for c in range(4):
                    o = (i % 2) * TILE + c * P
                    n = 4 * i + c
                    last = e.matmul(ps[0:E, o:o + P], gates[:, n * E:(n + 1) * E], prog.ident[:, :], is_transpose=True)
                last.then_inc(s_p, 1)
        marks_m, marks_ex = 12, 13
        marks_gates = marks_ex + 3 + 2 * int(np.log2(NB)) + 2 + 8
        phase(prog, dict(gpsimd=gpsimd, scalar=scalar, vector=vector, tensor=tensor))
        assert marks == dict(m=marks_m, ex=marks_ex, gates=marks_gates), marks


def run_experts(prog, h, w1, w2, b1, b2, gates, gt):
    x, mods = prog.x, prog.mods
    BT, BIAS = TILE // P, 32
    with ExitStack() as ctx:
        sb = lambda name, shape, dt=F32: prog.sb(ctx, f"y_{name}", shape, dt)
        sem = lambda n: prog.sem(f"y_{n}")
        hid = [sb(f"hid{i}", [P, HC, TILE]) for i in range(2)]
        acc = sb("acc", [P, BT, P])
        gfix = sb("gfix", [E, TILE])
        gtok = sb("gtok", [P, BT * E])
        up, act, down, ad = sem("up"), sem("gelu"), sem("down"), sem("added")
        gf, bp, ba, tp, xx = sem("gates"), sem("bias"), sem("bias_out"), sem("turned"), sem("x")
        at = lambda t, per, k: t * per + (BIAS + k)
        up_ps = [prog.pairs[i // 2][:, (i % 2) * TILE:(i % 2 + 1) * TILE] for i in range(4)]
        down_ps = [prog.pairs[2][:, i * TILE:(i + 1) * TILE] for i in range(2)]
        b_ps, t_ps = prog.banks

        def tensor(e):
            for s_ in (up, down, bp, tp):
                e.sem_inc(s_, BIAS)

            def down_of(t, k):
                e.wait_ge(act, at(t, 32, 4 * k + 4))
                e.wait_ge(ad, at(t, 32, 4 * (k - 1)))
                for c in range(BT):
                    for j in range(HC):
                        last = e.matmul(down_ps[k % 2][:, c * P:(c + 1) * P], hid[k % 2][:, j, c * P:(c + 1) * P],
                                        w2[:, k * HC + j, :], start=(j == 0), stop=(j == HC - 1))
                last.then_inc(down, 1)
            with e.Fori(0, NT) as t:
                for k in range(E):
                    for j in range(HC):
                        e.wait_ge(act, at(t, 32, 4 * k + j - 3))
                        e.matmul(up_ps[j], w1[:, k, j * P:(j + 1) * P], h[:, bass.ds(t * TILE, TILE)],
                                 start=True, stop=True).then_inc(up, 1)
                    if k == 0:
                        e.wait_ge(gf, at(t, 1, 1))
                        e.wait_ge(ba, at(t, 1, 0))
                        for c in range(BT):
                            last = e.matmul(b_ps[:, c * P:(c + 1) * P], gfix[:, c * P:(c + 1) * P], b2[:, :],
                                            start=True, stop=True)
                        last.then_inc(bp, 1)
                    else:
                        down_of(t, k - 1)
                down_of(t, E - 1)
                e.wait_ge(ad, at(t, 32, 32))
                e.wait_ge(xx, at(t, 1, 0))
                for c in range(BT):
                    last = e.matmul(t_ps[:, c * P:(c + 1) * P], acc[:, c, :], prog.ident[:, :], is_transpose=True)
                last.then_inc(tp, 1)

        def scalar(e):
            e.sem_inc(act, BIAS)
            with e.Fori(0, NT) as t:
                for k in range(E):
                    e.wait_ge(down, at(t, 8, k - 1))
                    for j in range(HC):
                        e.wait_ge(up, at(t, 32, 4 * k + j + 1))
                        e.activation(hid[k % 2][:, j, :], up_ps[j], ACT.Gelu_apprx_tanh,
                                     bias=b1[:, k * HC + j:k * HC + j + 1]).then_inc(act, 1)

        def vector(e):
            for s_ in (ad, gf, ba, xx):
                e.sem_inc(s_, BIAS)
            with e.Fori(0, NT) as t:
                e.wait_ge(bp, at(t, 1, 0))
                e.tensor_copy(gfix[:, :], gt[:, bass.ds(t * TILE, TILE)])
                e.wait_ge(ad, at(t, 32, 0))
                e.tensor_copy(gtok[:, :], gates[:, bass.ds(t * BT * E, BT * E)]).then_inc(gf, 1)
                e.wait_ge(bp, at(t, 1, 1))
                e.wait_ge(tp, at(t, 1, 0))
                e.tensor_copy(acc[:, :, :], b_ps.rearrange("p (c f) -> p c f", f=P)).then_inc(ba, 1)
                e.wait_ge(ba, at(t, 1, 1))
                e.wait_ge(gf, at(t, 1, 1))
                for k in range(E):
                    e.wait_ge(down, at(t, 8, k + 1))
                    e.wait_ge(ad, at(t, 32, 4 * k))
                    for c in range(BT):
                        e.scalar_tensor_tensor(out=acc[:, c, :], in0=down_ps[k % 2][:, c * P:(c + 1) * P],
                                               scalar=gtok[:, c * E + k:c * E + k + 1], in1=acc[:, c, :],
                                               op0=ALU.mult, op1=ALU.add).then_inc(ad, 1)
                e.wait_ge(tp, at(t, 1, 1))
                xb = x[:, bass.ds(t * TILE, TILE)]
                tb = lambda k: mods[:, 1, 5, bass.ds(t // 2, 1)]
                e.scalar_tensor_tensor(out=xb, in0=t_ps, scalar=tb(0), in1=xb, op0=ALU.mult,
                                       op1=ALU.add).then_inc(xx, 1)

        phase(prog, dict(scalar=scalar, vector=vector, tensor=tensor))


_COLUMNS = ("L0_attn_bq", "L1_attn_in_proj_b", "L1_ffn_b1")
_TRANSPOSED = ("L0_c", "L1_c", "L1_attn_in_proj_w", "L1_attn_out_w")


def laid_out(inputs):
    arrays = {}
    for name, value in inputs.items():
        value = np.asarray(value)
        if name == "L0_attn_x":
            name, value = "x", value.reshape(N, P).T
        elif name in _COLUMNS:
            value = value.reshape(-1, P).T
        elif name in _TRANSPOSED:
            value = value.T
        arrays[name] = np.ascontiguousarray(value)
    return arrays


def kernel(**inputs):
    import concourse.bacc as bacc
    from concourse.bass_utils import run_bass_kernel_spmd

    nc = bacc.Bacc("TRN2", target_bir_lowering=False, num_devices=1)
    arrays, aps = {}, {}
    for name, value in laid_out(inputs).items():
        arrays[f"in_{name}"] = value
        aps[name] = nc.dram_tensor(f"in_{name}", value.shape, mybir.dt.from_np(value.dtype), kind="ExternalInput").ap()
    out = nc.dram_tensor("out", (P, N), F32, kind="ExternalOutput").ap()
    build(nc, aps, out)
    result = run_bass_kernel_spmd(nc, [arrays], core_ids=[0]).results[0]["out"]
    return np.ascontiguousarray(np.asarray(result).T).reshape(B, S, P)
```
